# Optimizing a Trainium2 kernel written in Bass

```python
import numpy as np
import jax
import jax.numpy as jnp

def _softmax(x, axis=-1):
    return jax.nn.softmax(x, axis=axis)

def _gelu(x):
    return jax.nn.gelu(x, approximate=True)

def _silu(x):
    return jax.nn.silu(x)

def _sigmoid(x):
    return jax.nn.sigmoid(x)

def _layernorm(x, axis=-1, eps=1e-05):
    m = jnp.mean(x, axis=axis, keepdims=True)
    v = jnp.var(x, axis=axis, keepdims=True)
    return (x - m) / jnp.sqrt(v + eps)

def _scatter_add(tgt, idx, src, axis=0):
    return tgt.at[idx].add(src)

def _segment_sum(src, seg, n):
    return jax.ops.segment_sum(src, seg, n)
kernel_name = 'mk_dlrm_tower_d1_rec_r8_0976c5'

def setup_inputs(seed: int=0):
    np.random.seed(seed)
    _w = jnp.asarray

    def _rec_inputs():
        import jax
        import jax.numpy as jnp
        _tk = jax.random.key(seed)
        dense_ctx = jax.random.normal(jax.random.fold_in(_tk, 190), (512, 16), jnp.float32)
        ids = jnp.stack([jax.random.randint(jax.random.fold_in(_tk, 200 + f), (512,), 0, v, jnp.int32) for f, v in enumerate([125000, 1250, 12500, 1000, 1250, 1250, 1000, 1000, 1000, 1250, 1250, 12500, 1000, 1000, 1250, 1250, 12500, 1000, 1000, 12500, 1250, 1000, 1250, 1250, 1000, 1250, 1000])], axis=1)
        tbl_0 = 0.05 * jax.random.normal(jax.random.fold_in(_tk, 500 + 0), (125000, 128), jnp.float32)
        tbl_1 = 0.05 * jax.random.normal(jax.random.fold_in(_tk, 500 + 1), (1250, 128), jnp.float32)
        tbl_2 = 0.05 * jax.random.normal(jax.random.fold_in(_tk, 500 + 2), (12500, 128), jnp.float32)
        tbl_3 = 0.05 * jax.random.normal(jax.random.fold_in(_tk, 500 + 3), (1000, 128), jnp.float32)
        tbl_4 = 0.05 * jax.random.normal(jax.random.fold_in(_tk, 500 + 4), (1250, 128), jnp.float32)
        tbl_5 = 0.05 * jax.random.normal(jax.random.fold_in(_tk, 500 + 5), (1250, 128), jnp.float32)
        tbl_6 = 0.05 * jax.random.normal(jax.random.fold_in(_tk, 500 + 6), (1000, 128), jnp.float32)
        tbl_7 = 0.05 * jax.random.normal(jax.random.fold_in(_tk, 500 + 7), (1000, 128), jnp.float32)
        tbl_8 = 0.05 * jax.random.normal(jax.random.fold_in(_tk, 500 + 8), (1000, 128), jnp.float32)
        tbl_9 = 0.05 * jax.random.normal(jax.random.fold_in(_tk, 500 + 9), (1250, 128), jnp.float32)
        tbl_10 = 0.05 * jax.random.normal(jax.random.fold_in(_tk, 500 + 10), (1250, 128), jnp.float32)
        tbl_11 = 0.05 * jax.random.normal(jax.random.fold_in(_tk, 500 + 11), (12500, 128), jnp.float32)
        tbl_12 = 0.05 * jax.random.normal(jax.random.fold_in(_tk, 500 + 12), (1000, 128), jnp.float32)
        tbl_13 = 0.05 * jax.random.normal(jax.random.fold_in(_tk, 500 + 13), (1000, 128), jnp.float32)
        tbl_14 = 0.05 * jax.random.normal(jax.random.fold_in(_tk, 500 + 14), (1250, 128), jnp.float32)
        tbl_15 = 0.05 * jax.random.normal(jax.random.fold_in(_tk, 500 + 15), (1250, 128), jnp.float32)
        tbl_16 = 0.05 * jax.random.normal(jax.random.fold_in(_tk, 500 + 16), (12500, 128), jnp.float32)
        tbl_17 = 0.05 * jax.random.normal(jax.random.fold_in(_tk, 500 + 17), (1000, 128), jnp.float32)
        tbl_18 = 0.05 * jax.random.normal(jax.random.fold_in(_tk, 500 + 18), (1000, 128), jnp.float32)
        tbl_19 = 0.05 * jax.random.normal(jax.random.fold_in(_tk, 500 + 19), (12500, 128), jnp.float32)
        tbl_20 = 0.05 * jax.random.normal(jax.random.fold_in(_tk, 500 + 20), (1250, 128), jnp.float32)
        tbl_21 = 0.05 * jax.random.normal(jax.random.fold_in(_tk, 500 + 21), (1000, 128), jnp.float32)
        tbl_22 = 0.05 * jax.random.normal(jax.random.fold_in(_tk, 500 + 22), (1250, 128), jnp.float32)
        tbl_23 = 0.05 * jax.random.normal(jax.random.fold_in(_tk, 500 + 23), (1250, 128), jnp.float32)
        tbl_24 = 0.05 * jax.random.normal(jax.random.fold_in(_tk, 500 + 24), (1000, 128), jnp.float32)
        tbl_25 = 0.05 * jax.random.normal(jax.random.fold_in(_tk, 500 + 25), (1250, 128), jnp.float32)
        tbl_26 = 0.05 * jax.random.normal(jax.random.fold_in(_tk, 500 + 26), (1000, 128), jnp.float32)
        _rk = jax.random.fold_in(_tk, 7)
        W_top1 = 0.0521996 * jax.random.normal(jax.random.fold_in(_tk, 801), (367, 512), jnp.float32)
        W_top2 = 0.0441942 * jax.random.normal(jax.random.fold_in(_tk, 802), (512, 256), jnp.float32)
        W_top3 = 0.0625 * jax.random.normal(jax.random.fold_in(_tk, 803), (256, 1), jnp.float32)
        b_top1 = jnp.zeros((512,), jnp.float32)
        b_top2 = jnp.zeros((256,), jnp.float32)
        return (dense_ctx, ids, tbl_0, tbl_1, tbl_2, tbl_3, tbl_4, tbl_5, tbl_6, tbl_7, tbl_8, tbl_9, tbl_10, tbl_11, tbl_12, tbl_13, tbl_14, tbl_15, tbl_16, tbl_17, tbl_18, tbl_19, tbl_20, tbl_21, tbl_22, tbl_23, tbl_24, tbl_25, tbl_26, W_top1, b_top1, W_top2, b_top2, W_top3)
    dense_ctx, ids, tbl_0, tbl_1, tbl_2, tbl_3, tbl_4, tbl_5, tbl_6, tbl_7, tbl_8, tbl_9, tbl_10, tbl_11, tbl_12, tbl_13, tbl_14, tbl_15, tbl_16, tbl_17, tbl_18, tbl_19, tbl_20, tbl_21, tbl_22, tbl_23, tbl_24, tbl_25, tbl_26, W_top1, b_top1, W_top2, b_top2, W_top3 = _rec_inputs()

    def _L0_rec_setup():
        import jax, jax.numpy as jnp
        import numpy as np

        def _tri_indices(num_feas):
            return np.array([i * num_feas + j for j in range(1, num_feas) for i in range(j)], dtype=np.int32)
        key = jax.random.key(seed)
        batch, num_feas, embed_dim = (2048, 27, 128)
        inputs = jax.random.normal(key, (batch, num_feas, embed_dim), dtype=jnp.float32)
        return {'inputs': inputs, 'num_feas': num_feas}
    _L0_rec_all = _L0_rec_setup()
    _L0_rec_in = {k: v for k, v in _L0_rec_all.items() if k in ()}
    del _L0_rec_all
    return {'dense_ctx': dense_ctx, 'ids': ids, 'tbl_0': tbl_0, 'tbl_1': tbl_1, 'tbl_2': tbl_2, 'tbl_3': tbl_3, 'tbl_4': tbl_4, 'tbl_5': tbl_5, 'tbl_6': tbl_6, 'tbl_7': tbl_7, 'tbl_8': tbl_8, 'tbl_9': tbl_9, 'tbl_10': tbl_10, 'tbl_11': tbl_11, 'tbl_12': tbl_12, 'tbl_13': tbl_13, 'tbl_14': tbl_14, 'tbl_15': tbl_15, 'tbl_16': tbl_16, 'tbl_17': tbl_17, 'tbl_18': tbl_18, 'tbl_19': tbl_19, 'tbl_20': tbl_20, 'tbl_21': tbl_21, 'tbl_22': tbl_22, 'tbl_23': tbl_23, 'tbl_24': tbl_24, 'tbl_25': tbl_25, 'tbl_26': tbl_26, 'W_top1': W_top1, 'b_top1': b_top1, 'W_top2': W_top2, 'b_top2': b_top2, 'W_top3': W_top3}

def reference(dense_ctx, ids, tbl_0, tbl_1, tbl_2, tbl_3, tbl_4, tbl_5, tbl_6, tbl_7, tbl_8, tbl_9, tbl_10, tbl_11, tbl_12, tbl_13, tbl_14, tbl_15, tbl_16, tbl_17, tbl_18, tbl_19, tbl_20, tbl_21, tbl_22, tbl_23, tbl_24, tbl_25, tbl_26, W_top1, b_top1, W_top2, b_top2, W_top3):
    import jax
    import jax.numpy as jnp

    def _L0_rec_ref(inputs, num_feas):
        import jax, jax.numpy as jnp
        import numpy as np

        def _tri_indices(num_feas):
            return np.array([i * num_feas + j for j in range(1, num_feas) for i in range(j)], dtype=np.int32)
        dot = jnp.einsum('bnd,bmd->bnm', inputs, inputs)
        idx = jnp.asarray(_tri_indices(num_feas))
        flat = dot.reshape(inputs.shape[0], num_feas * num_feas)
        return flat[:, idx]
    e = jnp.stack([tbl_0[ids[:, 0]], tbl_1[ids[:, 1]], tbl_2[ids[:, 2]], tbl_3[ids[:, 3]], tbl_4[ids[:, 4]], tbl_5[ids[:, 5]], tbl_6[ids[:, 6]], tbl_7[ids[:, 7]], tbl_8[ids[:, 8]], tbl_9[ids[:, 9]], tbl_10[ids[:, 10]], tbl_11[ids[:, 11]], tbl_12[ids[:, 12]], tbl_13[ids[:, 13]], tbl_14[ids[:, 14]], tbl_15[ids[:, 15]], tbl_16[ids[:, 16]], tbl_17[ids[:, 17]], tbl_18[ids[:, 18]], tbl_19[ids[:, 19]], tbl_20[ids[:, 20]], tbl_21[ids[:, 21]], tbl_22[ids[:, 22]], tbl_23[ids[:, 23]], tbl_24[ids[:, 24]], tbl_25[ids[:, 25]], tbl_26[ids[:, 26]]], axis=1)
    z = _L0_rec_ref(e, 27)
    z = z.reshape(z.shape[0], -1)
    h = jnp.concatenate([z, dense_ctx], axis=1)
    h = jnp.maximum(h @ W_top1 + b_top1, 0.0)
    h = jnp.maximum(h @ W_top2 + b_top2, 0.0)
    y = h @ W_top3
    return y

_drawn_inputs = setup_inputs


def setup_inputs(seed=0):
    import zlib

    import numpy as np

    out = dict(_drawn_inputs(seed))
    spreads = {'b_top1': (0.0, 0.1), 'b_top2': (0.0, 0.1)}
    factors = {}
    for name, (base, spread) in spreads.items():
        noise = np.random.default_rng([zlib.crc32(name.encode()), seed]).standard_normal(out[name].shape)
        drawn = base * np.exp(spread * noise) if base else spread * noise
        out[name] = jnp.asarray(drawn.astype(out[name].dtype))
    for name, factor in factors.items():
        out[name] = (out[name] * factor).astype(out[name].dtype)
    return out
```

```python
import concourse.bass as bass
from concourse import mybir
from contextlib import ExitStack

TABLES = 27
DIM = 128
BATCH = 512
DENSE = 16
H1 = 512
H2 = 256
PAIRS = TABLES * (TABLES - 1) // 2


def pair_rows():
    order = []
    for k in range(1, (TABLES - 1) // 2 + 1):
        for i in range(TABLES):
            a, b = sorted((i, (i + k) % TABLES))
            order.append(b * (b - 1) // 2 + a)
    return order


def dlrm_tower(nc, dense_ctx, ids, tables, W1, b1, W2, b2, W3, out):
    fp32 = mybir.dt.float32
    i32 = mybir.dt.int32
    ALU = mybir.AluOpType
    ACT = mybir.ActivationFunctionType

    P = 128
    TILES = BATCH // P
    SLOT = 32
    J = P // SLOT
    GRAMS = P // J
    GROUP = 4
    GROUPS = [list(range(f, min(f + GROUP, TABLES))) for f in range(0, TABLES, GROUP)]
    NG = len(GROUPS)
    N_DVE = (NG + 1) // 2
    N_ACT = NG // 2
    PER_BANK = 4
    PER_ROUND = 2 * PER_BANK
    ROUNDS = GRAMS // PER_ROUND
    RING = (TABLES - 1) // 2
    GW = J * TABLES
    KC = (PAIRS + DENSE + 1 + P - 1) // P
    KLAST = PAIRS + DENSE + 1 - (KC - 1) * P
    U1, U2 = H1 // P, H2 // P

    ctx = ExitStack()
    with ctx:
        def sb(name, shape, dt=fp32):
            return ctx.enter_context(nc.sbuf_tensor(name, shape, dt))

        def ps(name, shape):
            return ctx.enter_context(nc.psum_tensor(name, shape, fp32))

        def sem(name):
            return ctx.enter_context(nc.semaphore(name))

        idx = sb("idx", [P, TILES, TABLES], i32)
        rows = sb("rows", [P, TILES, TABLES, DIM])
        cols = sb("cols", [P, BATCH, SLOT])
        ident = sb("ident", [P, P])
        ones = sb("ones", [P, P])
        gram = sb("gram", [P, 2, TABLES, GRAMS])
        turned = sb("turned", [P, 2, TABLES + RING, SLOT])
        feat = sb("feat", [P, TILES, KC * P])
        featT = sb("featT", [P, KC, P])
        w1 = sb("w1", [P, KC, H1])
        w2 = sb("w2", [P, U1, H2])
        w3 = sb("w3", [P, U2])
        b2c = sb("b2c", [P, U2])
        h1 = sb("h1", [P, U1, P])
        h2 = sb("h2", [P, U2, P])
        y = sb("y", [1, BATCH])

        psT = [ps(f"psT{i}", [P, GROUP, P]) for i in range(2)]
        psG = [ps(f"psG{i}", [P, 2, 512]) for i in range(2)]
        psA = ps("psA", [P, 512])
        psH = ps("psH", [P, U1, P])
        psZ = psA[:, 0:KC * P].rearrange("p (c b) -> p c b", c=KC)
        psH2 = psA[:, 0:H2].rearrange("p (c b) -> p c b", c=U2)
        psY = psA[0:1, H2:H2 + P]

        ids_in = sem("ids_in")
        dense_in = sem("dense_in")
        w1_in = sem("w1_in")
        w2_in = sem("w2_in")
        gathered = [sem(f"gathered{g}") for g in range(NG)]
        ones_set = sem("ones_set")
        ident_set = sem("ident_set")
        pads_set = sem("pads_set")
        group_turned = sem("group_turned")
        group_kept_dve = sem("group_kept_dve")
        group_kept_act = sem("group_kept_act")
        gram_done = sem("gram_done")
        gram_kept_dve = sem("gram_kept_dve")
        gram_kept_act = sem("gram_kept_act")
        blocks_turned = sem("blocks_turned")
        pairs_packed = sem("pairs_packed")
        feat_turned = sem("feat_turned")
        feat_kept = sem("feat_kept")
        h1_done = sem("h1_done")
        h1_kept = sem("h1_kept")
        h2_done = sem("h2_done")
        h2_kept = sem("h2_kept")
        y_done = sem("y_done")
        y_kept = sem("y_kept")
        y_out = sem("y_out")

        block = ctx.enter_context(nc.Block())

        def cols_of(t, g, n):
            b = t * P + g * J
            return cols[:, b:b + J, 0:n]

        @block.sync
        def _(sp):
            sp.dma_start(idx[:, :, :], ids.rearrange("(t p) f -> p t f", p=P)).then_inc(ids_in, 16)
            sp.dma_start(feat[:, :, PAIRS:PAIRS + DENSE],
                         dense_ctx.rearrange("(t p) f -> p t f", p=P)).then_inc(dense_in, 16)
            sp.dma_start(w1[:, 0:KC - 1, :],
                         W1[0:(KC - 1) * P, :].rearrange("(c p) n -> p c n", p=P)).then_inc(w1_in, 16)
            sp.dma_start(w1[0:KLAST - 1, KC - 1, :], W1[(KC - 1) * P:PAIRS + DENSE, :]).then_inc(w1_in, 16)
            sp.dma_start(w1[KLAST - 1:KLAST, KC - 1, :], b1).then_inc(w1_in, 16)
            sp.dma_start(w2[:, :, :], W2.rearrange("(c p) n -> p c n", p=P)).then_inc(w2_in, 16)
            sp.dma_start(w3[:, :], W3).then_inc(w2_in, 16)
            sp.dma_start(b2c[:, :], b2).then_inc(w2_in, 16)
            sp.wait_ge(y_kept, TILES)
            sp.dma_start(out, y[0:1, :]).then_inc(y_out, 16)
            sp.wait_ge(y_out, 16)

        @block.gpsimd
        def _(pool):
            nc.gpsimd.memset(ones[:, :], 1.0).then_inc(ones_set, 1)
            pool.wait_ge(ones_set, 1)
            nc.gpsimd.affine_select(out=ident[:, :], in_=ones[:, :], compare_op=ALU.is_equal, fill=0.0,
                                    base=0, pattern=[[-1, P]], channel_multiplier=1).then_inc(ident_set, 1)
            pool.wait_ge(ids_in, 16)
            for t in range(TILES):
                for g, group in enumerate(GROUPS):
                    if t > 0:
                        pool.wait_ge(gathered[g], 16 * len(group) * t)
                    for f in group:
                        pool.indirect_dma_start(rows[:, t, f, :], None, tables[f],
                                                bass.IndirectOffsetOnAxis(ap=idx[:, t, f:f + 1], axis=0)
                                                ).then_inc(gathered[g], 16)

        @block.tensor
        def _(pe):
            def turn_group(t, g):
                group = GROUPS[g]
                pe.wait_ge(gathered[g], 16 * len(group) * (t + 1))
                if g % 2 == 0 and t * N_DVE + g // 2 > 0:
                    pe.wait_ge(group_kept_dve, t * N_DVE + g // 2)
                if g % 2 == 1 and t * N_ACT + g // 2 > 0:
                    pe.wait_ge(group_kept_act, t * N_ACT + g // 2)
                for i, f in enumerate(group):
                    last = nc.tensor.transpose(psT[g % 2][:, i, :], rows[:, t, f, :], ident[:, :])
                last.then_inc(group_turned, 1)

            def grams(t):
                pe.wait_ge(group_kept_dve, N_DVE * (t + 1))
                pe.wait_ge(group_kept_act, N_ACT * (t + 1))
                for r in range(ROUNDS):
                    n = ROUNDS * t + r
                    if n >= 2:
                        pe.wait_ge(gram_kept_dve, n - 1)
                        pe.wait_ge(gram_kept_act, n - 1)
                    for s in range(PER_ROUND):
                        g = r * PER_ROUND + s
                        o = s % PER_BANK * GW
                        last = nc.tensor.matmul(psG[n % 2][:, s // PER_BANK, o:o + GW], cols_of(t, g, SLOT).rearrange("p j n -> p (j n)"),
                                                cols_of(t, g, TABLES), start=True, stop=True)
                    last.then_inc(gram_done, 1)

            def turn_feat(t):
                pe.wait_ge(pairs_packed, t + 1)
                if t > 0:
                    pe.wait_ge(y_kept, t)
                for c in range(KC):
                    last = nc.tensor.transpose(psZ[:, c, :], feat[:, t, c * P:(c + 1) * P], ident[:, :])
                last.then_inc(feat_turned, 1)

            def layer1(t):
                pe.wait_ge(feat_kept, t + 1)
                if t > 0:
                    pe.wait_ge(h1_kept, t)
                for u in range(U1):
                    for c in range(KC):
                        k = P if c < KC - 1 else KLAST
                        last = nc.tensor.matmul(psH[:, u, :], w1[0:k, c, u * P:(u + 1) * P], featT[0:k, c, :],
                                                start=(c == 0), stop=(c == KC - 1))
                last.then_inc(h1_done, 1)

            def layer2(t):
                pe.wait_ge(h1_kept, t + 1)
                for u in range(U2):
                    for c in range(U1):
                        last = nc.tensor.matmul(psH2[:, u, :], w2[:, c, u * P:(u + 1) * P], h1[:, c, :],
                                                start=(c == 0), stop=(c == U1 - 1))
                last.then_inc(h2_done, 1)

            def layer3(t):
                pe.wait_ge(h2_kept, t + 1)
                for c in range(U2):
                    last = nc.tensor.matmul(psY, w3[:, c:c + 1], h2[:, c, :], start=(c == 0), stop=(c == U2 - 1))
                last.then_inc(y_done, 1)

            pe.wait_ge(ident_set, 1)
            for t in range(TILES):
                turn_group(t, 0)
                turn_group(t, 1)
                if t == 0:
                    pe.wait_ge(pads_set, 1)
                    pe.wait_ge(dense_in, 16)
                if t > 0:
                    turn_feat(t - 1)
                turn_group(t, 2)
                if t == 1:
                    pe.wait_ge(w1_in, 48)
                    pe.wait_ge(w2_in, 48)
                if t > 0:
                    layer1(t - 1)
                turn_group(t, 3)
                if t > 0:
                    layer2(t - 1)
                turn_group(t, 4)
                if t > 0:
                    layer3(t - 1)
                for g in range(5, NG):
                    turn_group(t, g)
                grams(t)
            turn_feat(TILES - 1)
            layer1(TILES - 1)
            layer2(TILES - 1)
            layer3(TILES - 1)

        def group_cols(t, g):
            group = GROUPS[g]
            return cols[:, t * P:(t + 1) * P, group[0]:group[0] + len(group)]

        def group_ps(g):
            return psT[g % 2][:, 0:len(GROUPS[g]), :].rearrange("p f b -> p b f")

        def gram_block(n, j):
            return psG[n % 2][j * SLOT:(j + 1) * SLOT, :, 0:PER_BANK * GW].rearrange(
                "p a (g j m) -> p a g j m", g=PER_BANK, j=J)[:, :, :, j, :].rearrange("p a g m -> p m a g")

        def gram_dst(t, r, j):
            return gram[j * SLOT:(j + 1) * SLOT, t % 2, :, r * PER_ROUND:(r + 1) * PER_ROUND].rearrange(
                "p m (a g) -> p m a g", a=2)

        @block.vector
        def _(dve):
            nc.vector.memset(cols[:, :, TABLES:SLOT], 0.0)
            nc.vector.memset(feat[:, :, PAIRS + DENSE:PAIRS + DENSE + 1], 1.0)
            nc.vector.memset(feat[:, :, PAIRS + DENSE + 1:KC * P], 0.0).then_inc(pads_set, 1)

            def keep_group(t, g):
                dve.wait_ge(group_turned, t * NG + g + 1)
                nc.vector.tensor_copy(group_cols(t, g), group_ps(g)).then_inc(group_kept_dve, 1)

            def keep_grams(t):
                for r in range(ROUNDS):
                    n = ROUNDS * t + r
                    dve.wait_ge(gram_done, n + 1)
                    for j in (2, 3):
                        last = nc.vector.tensor_copy(gram_dst(t, r, j), gram_block(n, j))
                    last.then_inc(gram_kept_dve, 1)

            def turn_blocks(t):
                dve.wait_ge(gram_kept_dve, ROUNDS * (t + 1))
                dve.wait_ge(gram_kept_act, ROUNDS * (t + 1))
                if t >= 2:
                    dve.wait_ge(pairs_packed, t - 1)
                nc.vector.transpose(turned[:, t % 2, 0:TABLES, :].rearrange("p m n -> p (m n)"),
                                    gram[:, t % 2, :, :].rearrange("p m g -> p (m g)"))
                nc.vector.transpose(turned[:, t % 2, TABLES:TABLES + RING, :].rearrange("p m n -> p (m n)"),
                                    gram[:, t % 2, 0:RING, :].rearrange("p m g -> p (m g)")
                                    ).then_inc(blocks_turned, 1)

            def keep_feat(t):
                dve.wait_ge(feat_turned, t + 1)
                if t > 0:
                    dve.wait_ge(h1_done, t)
                nc.vector.tensor_copy(featT[:, :, :], psZ).then_inc(feat_kept, 1)

            def keep_y(t):
                dve.wait_ge(y_done, t + 1)
                nc.vector.tensor_copy(y[0:1, t * P:(t + 1) * P], psY).then_inc(y_kept, 1)

            for t in range(TILES):
                keep_group(t, 0)
                if t > 0:
                    keep_feat(t - 1)
                keep_group(t, 2)
                keep_group(t, 4)
                if t > 0:
                    keep_y(t - 1)
                keep_group(t, 6)
                keep_grams(t)
                turn_blocks(t)
            keep_feat(TILES - 1)
            keep_y(TILES - 1)

        @block.scalar
        def _(act):
            def keep_group(t, g):
                act.wait_ge(group_turned, t * NG + g + 1)
                nc.scalar.copy(group_cols(t, g), group_ps(g)).then_inc(group_kept_act, 1)

            def keep_grams(t):
                if t >= 2:
                    act.wait_ge(blocks_turned, t - 1)
                for r in range(ROUNDS):
                    n = ROUNDS * t + r
                    act.wait_ge(gram_done, n + 1)
                    for j in (0, 1):
                        last = nc.scalar.copy(gram_dst(t, r, j), gram_block(n, j))
                    last.then_inc(gram_kept_act, 1)

            def pack_pairs(t):
                act.wait_ge(blocks_turned, t + 1)
                ring = turned[:, t % 2, :, :].rearrange("p m n -> p (m n)")
                src = bass.AP(ring.tensor, ring.offset + SLOT, [ring.ap[0], [SLOT, RING], [SLOT + 1, TABLES]])
                nc.scalar.copy(feat[:, t, 0:PAIRS].rearrange("p (k i) -> p k i", k=RING), src
                               ).then_inc(pairs_packed, 1)

            def keep_h1(t):
                act.wait_ge(h1_done, t + 1)
                if t > 0:
                    act.wait_ge(h2_done, t)
                nc.scalar.activation(h1[:, :, :], psH[:, :, :], ACT.Relu).then_inc(h1_kept, 1)

            def keep_h2(t):
                act.wait_ge(h2_done, t + 1)
                if t > 0:
                    act.wait_ge(y_done, t)
                for u in range(U2):
                    last = nc.scalar.activation(h2[:, u, :], psH2[:, u, :], ACT.Relu, bias=b2c[:, u:u + 1])
                last.then_inc(h2_kept, 1)

            for t in range(TILES):
                if t > 0:
                    pack_pairs(t - 1)
                keep_group(t, 1)
                if t > 0:
                    keep_h1(t - 1)
                keep_group(t, 3)
                if t == 1:
                    act.wait_ge(w2_in, 48)
                if t > 0:
                    keep_h2(t - 1)
                keep_group(t, 5)
                keep_grams(t)
            pack_pairs(TILES - 1)
            keep_h1(TILES - 1)
            keep_h2(TILES - 1)


def kernel(**inputs):
    import numpy as np
    import concourse.bacc as bacc
    from concourse.bass_utils import run_bass_kernel_spmd

    nc = bacc.Bacc("TRN2", target_bir_lowering=False, num_devices=1)
    arrays = {}

    def given(name, a):
        arrays[name] = np.ascontiguousarray(a)
        return nc.dram_tensor(name, arrays[name].shape, mybir.dt.from_np(arrays[name].dtype),
                              kind="ExternalInput").ap()

    w = np.asarray(inputs["W_top1"])
    w = np.concatenate([w[np.array(pair_rows())], w[PAIRS:]], axis=0)
    ids = np.asarray(inputs["ids"]).reshape(-1, 4, 32, TABLES).transpose(0, 2, 1, 3).reshape(BATCH, TABLES)
    args = [given("dense_dram", inputs["dense_ctx"]), given("ids_dram", ids),
            [given(f"table{f}_dram", inputs[f"tbl_{f}"]) for f in range(TABLES)],
            given("w1_dram", w), given("b1_dram", np.asarray(inputs["b_top1"]).reshape(1, H1)),
            given("w2_dram", inputs["W_top2"]),
            given("b2_dram", np.asarray(inputs["b_top2"]).reshape(H2 // 128, 128).T),
            given("w3_dram", np.asarray(inputs["W_top3"]).reshape(H2 // 128, 128).T)]
    out = nc.dram_tensor("y_dram", (1, BATCH), mybir.dt.float32, kind="ExternalOutput").ap()
    dlrm_tower(nc, *args[:3], args[3], args[4], args[5], args[6], args[7], out)
    r = run_bass_kernel_spmd(nc, [arrays], core_ids=[0])
    return r.results[0]["y_dram"].reshape(BATCH, 1)
```

```python
import concourse.bass as bass
from concourse import mybir
from contextlib import ExitStack

TABLES = 27
DIM = 128
BATCH = 512
DENSE = 16
H1 = 512
H2 = 256
PAIRS = TABLES * (TABLES - 1) // 2
SMALL = 1000
ONEHOT = [3, 6, 7, 8, 12, 13, 17, 18]
GATHER = [f for f in range(TABLES) if f not in ONEHOT]
SLOTS = GATHER + ONEHOT


def pair_rows():
    order = []
    for k in range(1, (TABLES - 1) // 2 + 1):
        for i in range(TABLES):
            a, b = sorted((SLOTS[i], SLOTS[(i + k) % TABLES]))
            order.append(b * (b - 1) // 2 + a)
    return order


def dlrm_tower(nc, dense_ctx, ids, onehot_ids, tables, W1, b1, W2, b2, W3, out):
    fp32 = mybir.dt.float32
    fp32r = mybir.dt.float32r
    i32 = mybir.dt.int32
    ALU = mybir.AluOpType
    ACT = mybir.ActivationFunctionType

    P = 128
    TILES = BATCH // P
    SLOT = 32
    J = P // SLOT
    GRAMS = P // J
    GROUP = 4
    NGATHER, NONE = len(GATHER), len(ONEHOT)
    GROUPS = [list(range(f, min(f + GROUP, NGATHER))) for f in range(0, NGATHER, GROUP)]
    V = SMALL // 8
    CHUNKS = SMALL // V
    RING = 3
    BY_DVE = 5
    BY_ACT = CHUNKS - BY_DVE
    ROW_TILES = 3
    NG = len(GROUPS)
    N_DVE = (NG + 1) // 2
    N_ACT = NG // 2
    PER_BANK = 4
    PER_ROUND = 2 * PER_BANK
    ROUNDS = GRAMS // PER_ROUND
    REACH = (TABLES - 1) // 2
    GW = J * TABLES
    KC = (PAIRS + DENSE + 1 + P - 1) // P
    KLAST = PAIRS + DENSE + 1 - (KC - 1) * P
    U1, U2 = H1 // P, H2 // P

    ctx = ExitStack()
    with ctx:
        def sb(name, shape, dt=fp32):
            return ctx.enter_context(nc.sbuf_tensor(name, shape, dt))

        def ps(name, shape):
            return ctx.enter_context(nc.psum_tensor(name, shape, fp32))

        def sem(name):
            return ctx.enter_context(nc.semaphore(name))

        idx = sb("idx", [P, TILES, TABLES], i32)
        rows = sb("rows", [P, ROW_TILES, NGATHER, DIM])
        idsI = sb("idsI", [NONE, BATCH], i32)
        idsR = sb("idsR", [NONE, BATCH], fp32r)
        pick = sb("pick", [NONE, NONE], fp32r)
        rowI = sb("rowI", [V, CHUNKS], i32)
        row_no = sb("row_no", [V, CHUNKS])
        row_neg = sb("row_neg", [V, CHUNKS])
        small = sb("small", [V, RING, CHUNKS, DIM])
        high = sb("high", [V, 2, CHUNKS, DIM], fp32r)
        low = sb("low", [V, 2, CHUNKS, DIM], fp32r)
        hot_dve = sb("hot_dve", [V, 2, BY_DVE, BATCH], fp32r)
        hot_act = sb("hot_act", [V, 2, BY_ACT, BATCH], fp32r)
        away = sb("away", [V, BY_ACT, BATCH])
        cols = sb("cols", [P, BATCH, SLOT])
        ident = sb("ident", [P, P])
        ones = sb("ones", [P, P])
        gram = sb("gram", [P, 2, TABLES, GRAMS])
        turned = sb("turned", [P, 2, TABLES + REACH, SLOT])
        feat = sb("feat", [P, TILES, KC * P])
        featT = sb("featT", [P, KC, P])
        w1 = sb("w1", [P, KC, H1])
        w2 = sb("w2", [P, U1, H2])
        w3 = sb("w3", [P, U2])
        b2c = sb("b2c", [P, U2])
        h1 = sb("h1", [P, U1, P])
        h2 = sb("h2", [P, U2, P])
        y = sb("y", [1, BATCH])

        psT = [ps(f"psT{i}", [P, GROUP, P]) for i in range(2)]
        psG = [ps(f"psG{i}", [P, 2, 512]) for i in range(2)]
        psA = ps("psA", [P, 512])
        psH = ps("psH", [P, U1, P])
        psZ = psA[:, 0:KC * P].rearrange("p (c b) -> p c b", c=KC)
        psH2 = psA[:, 0:H2].rearrange("p (c b) -> p c b", c=U2)
        psY = psA[0:1, H2:H2 + P]

        def ps_ids_dve(i):
            return psG[0][:, i % 2, :]

        def ps_ids_act(i):
            return psA[:, :] if i % 2 else psH[:, :, :].rearrange("p u b -> p (u b)")

        def ps_lookup(i):
            return psG[1][:, i % 2, :]

        ids_in = sem("ids_in")
        dense_in = sem("dense_in")
        w1_in = sem("w1_in")
        w2_in = sem("w2_in")
        onehot_ids_in = sem("onehot_ids_in")
        small_in = [sem(f"small_in{i}") for i in range(RING)]
        row_ids = sem("row_ids")
        row_nos = sem("row_nos")
        ids_rounded = sem("ids_rounded")
        ids_spread = sem("ids_spread")
        high_made = sem("high_made")
        low_made = sem("low_made")
        hot_made_dve = sem("hot_made_dve")
        hot_made_act = sem("hot_made_act")
        away_made = sem("away_made")
        looked_up = sem("looked_up")
        lookup_kept = sem("lookup_kept")
        gathered = [sem(f"gathered{g}") for g in range(NG)]
        ones_set = sem("ones_set")
        ident_set = sem("ident_set")
        pads_set = sem("pads_set")
        group_turned = sem("group_turned")
        group_kept_dve = sem("group_kept_dve")
        group_kept_act = sem("group_kept_act")
        gram_done = sem("gram_done")
        gram_kept_dve = sem("gram_kept_dve")
        gram_kept_act = sem("gram_kept_act")
        blocks_turned = sem("blocks_turned")
        pairs_packed = sem("pairs_packed")
        feat_turned = sem("feat_turned")
        feat_kept = sem("feat_kept")
        h1_done = sem("h1_done")
        h1_kept = sem("h1_kept")
        h2_done = sem("h2_done")
        h2_kept = sem("h2_kept")
        y_done = sem("y_done")
        y_kept = sem("y_kept")
        y_out = sem("y_out")

        block = ctx.enter_context(nc.Block())

        EARLY = 3

        def cols_of(t, g, n):
            b = t * P + g * J
            return cols[:, b:b + J, 0:n]

        @block.sync
        def _(sp):
            sp.dma_start(idx[:, :, :], ids.rearrange("(t p) f -> p t f", p=P)).then_inc(ids_in, 16)
            sp.dma_start(idsI[:, :], onehot_ids).then_inc(onehot_ids_in, 16)

            def load_small(i):
                sp.dma_start(small[:, i % RING, :, :], tables[ONEHOT[i]].rearrange("(p c) d -> p c d", p=V)
                             ).then_inc(small_in[i % RING], 16)

            for i in range(RING):
                load_small(i)
            sp.dma_start(feat[:, :, PAIRS:PAIRS + DENSE],
                         dense_ctx.rearrange("(t p) f -> p t f", p=P)).then_inc(dense_in, 16)
            sp.dma_start(w1[:, 0:KC - 1, :],
                         W1[0:(KC - 1) * P, :].rearrange("(c p) n -> p c n", p=P)).then_inc(w1_in, 16)
            sp.dma_start(w1[0:KLAST - 1, KC - 1, :], W1[(KC - 1) * P:PAIRS + DENSE, :]).then_inc(w1_in, 16)
            sp.dma_start(w1[KLAST - 1:KLAST, KC - 1, :], b1).then_inc(w1_in, 16)
            sp.dma_start(w2[:, :, :], W2.rearrange("(c p) n -> p c n", p=P)).then_inc(w2_in, 16)
            sp.dma_start(w3[:, :], W3).then_inc(w2_in, 16)
            sp.dma_start(b2c[:, :], b2).then_inc(w2_in, 16)
            for i in range(RING, NONE):
                sp.wait_ge(low_made, i - RING + 1)
                load_small(i)
            sp.wait_ge(y_kept, TILES)
            sp.dma_start(out, y[0:1, :]).then_inc(y_out, 16)
            sp.wait_ge(y_out, 16)

        @block.gpsimd
        def _(pool):
            nc.gpsimd.memset(ones[:, :], 1.0).then_inc(ones_set, 1)
            pool.wait_ge(ones_set, 1)
            nc.gpsimd.affine_select(out=ident[:, :], in_=ones[:, :], compare_op=ALU.is_equal, fill=0.0,
                                    base=0, pattern=[[-1, P]], channel_multiplier=1).then_inc(ident_set, 1)
            nc.gpsimd.iota(rowI[:, :], pattern=[[1, CHUNKS]], base=0, channel_multiplier=CHUNKS
                           ).then_inc(row_ids, 1)
            pool.wait_ge(ids_in, 16)
            for t in range(TILES):
                for g, group in enumerate(GROUPS):
                    if t > 0:
                        pool.wait_ge(gathered[g], 16 * len(group) * t)
                    if t >= ROW_TILES:
                        pool.wait_ge(group_turned, (t - ROW_TILES) * NG + g + 1)
                    for s in group:
                        f = GATHER[s]
                        pool.indirect_dma_start(rows[:, t % ROW_TILES, s, :], None, tables[f],
                                                bass.IndirectOffsetOnAxis(ap=idx[:, t, f:f + 1], axis=0)
                                                ).then_inc(gathered[g], 16)

        @block.tensor
        def _(pe):
            def turn_group(t, g):
                group = GROUPS[g]
                pe.wait_ge(gathered[g], 16 * len(group) * (t + 1))
                if g % 2 == 0 and t * N_DVE + g // 2 > 0:
                    pe.wait_ge(group_kept_dve, t * N_DVE + g // 2)
                if g % 2 == 1 and t * N_ACT + g // 2 > 0:
                    pe.wait_ge(group_kept_act, t * N_ACT + g // 2)
                for i, f in enumerate(group):
                    last = nc.tensor.transpose(psT[g % 2][:, i, :], rows[:, t % ROW_TILES, f, :], ident[:, :])
                last.then_inc(group_turned, 1)

            def spread_ids(i):
                row = pick[:, i:i + 1]
                row = bass.AP(row.tensor, row.offset, [row.ap[0], [0, P]])
                nc.tensor.matmul(ps_ids_dve(i), row, idsR[:, :], start=True, stop=True)
                nc.tensor.matmul(ps_ids_act(i), row, idsR[:, :], start=True, stop=True).then_inc(ids_spread, 1)

            def lookup(i):
                pe.wait_ge(low_made, i + 1)
                if i >= 2:
                    pe.wait_ge(lookup_kept, i - 1)
                for c in range(CHUNKS):
                    if c < BY_DVE:
                        pe.wait_ge(hot_made_dve, i * BY_DVE + c + 1)
                        hot = hot_dve[:, i % 2, c, :]
                    else:
                        pe.wait_ge(hot_made_act, i * BY_ACT + c - BY_DVE + 1)
                        hot = hot_act[:, i % 2, c - BY_DVE, :]
                    nc.tensor.matmul(ps_lookup(i), high[:, i % 2, c, :], hot, start=(c == 0), stop=False)
                    last = nc.tensor.matmul(ps_lookup(i), low[:, i % 2, c, :], hot, start=False,
                                            stop=(c == CHUNKS - 1))
                last.then_inc(looked_up, 1)

            def gram_round(t, r):
                if r == 0:
                    if t == 0:
                        pe.wait_ge(lookup_kept, NONE)
                    pe.wait_ge(group_kept_dve, N_DVE * (t + 1))
                    pe.wait_ge(group_kept_act, N_ACT * (t + 1))
                n = ROUNDS * t + r
                if n >= 2:
                    pe.wait_ge(gram_kept_dve, n - 1)
                    pe.wait_ge(gram_kept_act, n - 1)
                for s in range(PER_ROUND):
                    g = r * PER_ROUND + s
                    o = s % PER_BANK * GW
                    last = nc.tensor.matmul(psG[n % 2][:, s // PER_BANK, o:o + GW],
                                            cols_of(t, g, SLOT).rearrange("p j n -> p (j n)"),
                                            cols_of(t, g, TABLES), start=True, stop=True)
                last.then_inc(gram_done, 1)

            def turn_feat(t):
                pe.wait_ge(pairs_packed, t + 1)
                if t > 0:
                    pe.wait_ge(y_kept, t)
                for c in range(KC):
                    last = nc.tensor.transpose(psZ[:, c, :], feat[:, t, c * P:(c + 1) * P], ident[:, :])
                last.then_inc(feat_turned, 1)

            def layer1(t):
                pe.wait_ge(feat_kept, t + 1)
                if t > 0:
                    pe.wait_ge(h1_kept, t)
                for u in range(U1):
                    for c in range(KC):
                        k = P if c < KC - 1 else KLAST
                        last = nc.tensor.matmul(psH[:, u, :], w1[0:k, c, u * P:(u + 1) * P], featT[0:k, c, :],
                                                start=(c == 0), stop=(c == KC - 1))
                last.then_inc(h1_done, 1)

            def layer2(t):
                pe.wait_ge(h1_kept, t + 1)
                for u in range(U2):
                    for c in range(U1):
                        last = nc.tensor.matmul(psH2[:, u, :], w2[:, c, u * P:(u + 1) * P], h1[:, c, :],
                                                start=(c == 0), stop=(c == U1 - 1))
                last.then_inc(h2_done, 1)

            def layer3(t):
                pe.wait_ge(h2_kept, t + 1)
                for c in range(U2):
                    last = nc.tensor.matmul(psY, w3[:, c:c + 1], h2[:, c, :], start=(c == 0), stop=(c == U2 - 1))
                last.then_inc(y_done, 1)

            pe.wait_ge(ids_rounded, 2)
            spread_ids(0)
            spread_ids(1)
            pe.wait_ge(ident_set, 1)
            for i in range(NONE):
                lookup(i)
                if i + 2 < NONE:
                    spread_ids(i + 2)
                if i < NG + EARLY:
                    turn_group(i // NG, i % NG)
            pe.wait_ge(pads_set, 1)
            pe.wait_ge(dense_in, 16)
            pe.wait_ge(w1_in, 48)
            pe.wait_ge(w2_in, 48)
            for t in range(TILES - 1):
                if t > 0:
                    turn_group(t + 1, 0)
                gram_round(t, 0)
                if t > 1:
                    layer3(t - 2)
                if t > 0:
                    turn_group(t + 1, 1)
                gram_round(t, 1)
                if t > 0:
                    turn_feat(t - 1)
                    turn_group(t + 1, 2)
                gram_round(t, 2)
                if t > 0:
                    layer1(t - 1)
                turn_group(t + 1, 3)
                gram_round(t, 3)
                if t > 0:
                    layer2(t - 1)
                turn_group(t + 1, 4)
            t = TILES - 1
            gram_round(t, 0)
            layer3(t - 2)
            gram_round(t, 1)
            turn_feat(t - 1)
            gram_round(t, 2)
            gram_round(t, 3)
            layer1(t - 1)
            layer2(t - 1)
            layer3(t - 1)
            turn_feat(t)
            layer1(t)
            layer2(t)
            layer3(t)

        def group_cols(t, g):
            group = GROUPS[g]
            return cols[:, t * P:(t + 1) * P, group[0]:group[0] + len(group)]

        def group_ps(g):
            return psT[g % 2][:, 0:len(GROUPS[g]), :].rearrange("p f b -> p b f")

        def gram_block(n, j):
            return psG[n % 2][j * SLOT:(j + 1) * SLOT, :, 0:PER_BANK * GW].rearrange(
                "p a (g j m) -> p a g j m", g=PER_BANK, j=J)[:, :, :, j, :].rearrange("p a g m -> p m a g")

        def gram_dst(t, r, j):
            return gram[j * SLOT:(j + 1) * SLOT, t % 2, :, r * PER_ROUND:(r + 1) * PER_ROUND].rearrange(
                "p m (a g) -> p m a g", a=2)

        @block.vector
        def _(dve):
            nc.vector.memset(cols[:, :, TABLES:SLOT], 0.0)
            nc.vector.memset(feat[:, :, PAIRS + DENSE:PAIRS + DENSE + 1], 1.0)
            nc.vector.memset(feat[:, :, PAIRS + DENSE + 1:KC * P], 0.0).then_inc(pads_set, 1)

            def keep_group(t, g):
                dve.wait_ge(group_turned, t * NG + g + 1)
                nc.vector.tensor_copy(group_cols(t, g), group_ps(g)).then_inc(group_kept_dve, 1)

            def keep_round(t, r):
                n = ROUNDS * t + r
                dve.wait_ge(gram_done, n + 1)
                for j in (2, 3):
                    last = nc.vector.tensor_copy(gram_dst(t, r, j), gram_block(n, j))
                last.then_inc(gram_kept_dve, 1)

            def turn_blocks(t):
                dve.wait_ge(gram_kept_dve, ROUNDS * (t + 1))
                dve.wait_ge(gram_kept_act, ROUNDS * (t + 1))
                if t >= 2:
                    dve.wait_ge(pairs_packed, t - 1)
                nc.vector.transpose(turned[:, t % 2, 0:TABLES, :].rearrange("p m n -> p (m n)"),
                                    gram[:, t % 2, :, :].rearrange("p m g -> p (m g)"))
                nc.vector.transpose(turned[:, t % 2, TABLES:TABLES + REACH, :].rearrange("p m n -> p (m n)"),
                                    gram[:, t % 2, 0:REACH, :].rearrange("p m g -> p (m g)")
                                    ).then_inc(blocks_turned, 1)

            def keep_feat(t):
                dve.wait_ge(feat_turned, t + 1)
                if t > 0:
                    dve.wait_ge(h1_done, t)
                nc.vector.tensor_copy(featT[:, :, :], psZ).then_inc(feat_kept, 1)

            def keep_y(t):
                dve.wait_ge(y_done, t + 1)
                nc.vector.tensor_copy(y[0:1, t * P:(t + 1) * P], psY).then_inc(y_kept, 1)

            def split_low(i):
                dve.wait_ge(high_made, i + 1)
                nc.vector.tensor_tensor(low[:, i % 2, :, :], small[:, i % RING, :, :],
                                        high[:, i % 2, :, :].bitcast(fp32), ALU.subtract
                                        ).then_inc(low_made, 1)

            def make_hot(i):
                dve.wait_ge(ids_spread, i + 1)
                if i >= 2:
                    dve.wait_ge(looked_up, i - 1)
                for c in range(BY_DVE):
                    nc.vector.tensor_scalar(hot_dve[:, i % 2, c, :], ps_ids_dve(i)[0:V, :], row_no[:, c:c + 1],
                                            None, ALU.is_equal).then_inc(hot_made_dve, 1)

            dve.wait_ge(row_ids, 1)
            nc.vector.tensor_copy(row_no[:, :], rowI[:, :])
            nc.vector.tensor_scalar(row_neg[:, :], rowI[:, :], -1.0, None, ALU.mult).then_inc(row_nos, 1)
            dve.wait_ge(row_nos, 1)
            dve.wait_ge(ident_set, 1)
            nc.vector.tensor_copy(pick[:, :], ident[0:NONE, 0:NONE]).then_inc(ids_rounded, 1)
            dve.wait_ge(onehot_ids_in, 16)
            nc.vector.tensor_copy(idsR[:, :], idsI[:, :]).then_inc(ids_rounded, 1)
            make_hot(0)
            split_low(0)
            for i in range(NONE):
                if i + 1 < NONE:
                    split_low(i + 1)
                    make_hot(i + 1)
                if i < NG + EARLY and i % NG % 2 == 0:
                    keep_group(i // NG, i % NG)
            for t in range(TILES):
                more = t + 1 < TILES
                if t > 0 and more:
                    keep_group(t + 1, 0)
                keep_round(t, 0)
                if t > 1:
                    keep_y(t - 2)
                keep_round(t, 1)
                if t > 0:
                    keep_feat(t - 1)
                    if more:
                        keep_group(t + 1, 2)
                keep_round(t, 2)
                keep_round(t, 3)
                if more:
                    keep_group(t + 1, 4)
                turn_blocks(t)
            keep_y(TILES - 2)
            keep_feat(TILES - 1)
            keep_y(TILES - 1)

        @block.scalar
        def _(act):
            def keep_group(t, g):
                act.wait_ge(group_turned, t * NG + g + 1)
                nc.scalar.copy(group_cols(t, g), group_ps(g)).then_inc(group_kept_act, 1)

            def keep_round(t, r):
                if r == 0 and t >= 2:
                    act.wait_ge(blocks_turned, t - 1)
                n = ROUNDS * t + r
                act.wait_ge(gram_done, n + 1)
                for j in (0, 1):
                    last = nc.scalar.copy(gram_dst(t, r, j), gram_block(n, j))
                last.then_inc(gram_kept_act, 1)

            def pack_pairs(t):
                act.wait_ge(blocks_turned, t + 1)
                ring = turned[:, t % 2, :, :].rearrange("p m n -> p (m n)")
                src = bass.AP(ring.tensor, ring.offset + SLOT, [ring.ap[0], [SLOT, REACH], [SLOT + 1, TABLES]])
                nc.scalar.copy(feat[:, t, 0:PAIRS].rearrange("p (k i) -> p k i", k=REACH), src
                               ).then_inc(pairs_packed, 1)

            def keep_h1(t):
                act.wait_ge(h1_done, t + 1)
                if t > 0:
                    act.wait_ge(h2_done, t)
                nc.scalar.activation(h1[:, :, :], psH[:, :, :], ACT.Relu).then_inc(h1_kept, 1)

            def keep_h2(t):
                act.wait_ge(h2_done, t + 1)
                if t > 0:
                    act.wait_ge(y_done, t)
                for u in range(U2):
                    last = nc.scalar.activation(h2[:, u, :], psH2[:, u, :], ACT.Relu, bias=b2c[:, u:u + 1])
                last.then_inc(h2_kept, 1)

            def split_high(i):
                act.wait_ge(small_in[i % RING], 16 * (i // RING + 1))
                if i >= 2:
                    act.wait_ge(looked_up, i - 1)
                nc.scalar.copy(high[:, i % 2, :, :], small[:, i % RING, :, :]).then_inc(high_made, 1)

            def make_hot(i):
                act.wait_ge(ids_spread, i + 1)
                if i > 0:
                    act.wait_ge(hot_made_act, i * BY_ACT)
                for c in range(BY_ACT):
                    nc.scalar.activation(away[:, c, :], ps_ids_act(i)[0:V, :], ACT.Abs,
                                         bias=row_neg[:, BY_DVE + c:BY_DVE + c + 1]).then_inc(away_made, 1)
                if i >= 2:
                    act.wait_ge(looked_up, i - 1)
                for c in range(BY_ACT):
                    act.wait_ge(away_made, i * BY_ACT + c + 1)
                    nc.scalar.activation(hot_act[:, i % 2, c, :], away[:, c, :], ACT.Relu, bias=1.0, scale=-1.0
                                         ).then_inc(hot_made_act, 1)

            def keep_lookup(i):
                act.wait_ge(looked_up, i + 1)
                nc.scalar.copy(cols[:, :, NGATHER + i], ps_lookup(i)).then_inc(lookup_kept, 1)

            act.wait_ge(row_nos, 1)
            split_high(0)
            make_hot(0)
            for i in range(NONE):
                if i + 1 < NONE:
                    split_high(i + 1)
                    make_hot(i + 1)
                keep_lookup(i)
                if i < NG + EARLY and i % NG % 2 == 1:
                    keep_group(i // NG, i % NG)
            act.wait_ge(w2_in, 48)
            for t in range(TILES - 1):
                keep_round(t, 0)
                if t > 0:
                    keep_group(t + 1, 1)
                keep_round(t, 1)
                keep_round(t, 2)
                if t > 0:
                    keep_h1(t - 1)
                keep_group(t + 1, 3)
                keep_round(t, 3)
                if t > 0:
                    keep_h2(t - 1)
                pack_pairs(t)
            t = TILES - 1
            for r in range(ROUNDS):
                keep_round(t, r)
            keep_h1(t - 1)
            keep_h2(t - 1)
            pack_pairs(t)
            keep_h1(t)
            keep_h2(t)


def kernel(**inputs):
    import numpy as np
    import concourse.bacc as bacc
    from concourse.bass_utils import run_bass_kernel_spmd

    nc = bacc.Bacc("TRN2", target_bir_lowering=False, num_devices=1)
    arrays = {}

    def given(name, a):
        arrays[name] = np.ascontiguousarray(a)
        return nc.dram_tensor(name, arrays[name].shape, mybir.dt.from_np(arrays[name].dtype),
                              kind="ExternalInput").ap()

    w = np.asarray(inputs["W_top1"])
    w = np.concatenate([w[np.array(pair_rows())], w[PAIRS:]], axis=0)
    ids = np.asarray(inputs["ids"]).reshape(-1, 4, 32, TABLES).transpose(0, 2, 1, 3).reshape(BATCH, TABLES)
    args = [given("dense_dram", inputs["dense_ctx"]), given("ids_dram", ids),
            given("onehot_ids_dram", ids[:, ONEHOT].T),
            [given(f"table{f}_dram", inputs[f"tbl_{f}"]) for f in range(TABLES)],
            given("w1_dram", w), given("b1_dram", np.asarray(inputs["b_top1"]).reshape(1, H1)),
            given("w2_dram", inputs["W_top2"]),
            given("b2_dram", np.asarray(inputs["b_top2"]).reshape(H2 // 128, 128).T),
            given("w3_dram", np.asarray(inputs["W_top3"]).reshape(H2 // 128, 128).T)]
    out = nc.dram_tensor("y_dram", (1, BATCH), mybir.dt.float32, kind="ExternalOutput").ap()
    dlrm_tower(nc, *args, out)
    r = run_bass_kernel_spmd(nc, [arrays], core_ids=[0])
    return r.results[0]["y_dram"].reshape(BATCH, 1)
```

```python
import concourse.bass as bass
from concourse import mybir
from contextlib import ExitStack

TABLES = 27
DIM = 128
BATCH = 512
DENSE = 16
H1 = 512
H2 = 256
PAIRS = TABLES * (TABLES - 1) // 2
CHUNKS = 8
ONEHOT = [3, 6, 7, 8, 12, 13, 17, 18, 21, 24]
GATHER = [f for f in range(TABLES) if f not in ONEHOT]
SLOTS = GATHER + ONEHOT


def pair_rows():
    order = []
    for k in range(1, (TABLES - 1) // 2 + 1):
        for i in range(TABLES):
            a, b = sorted((SLOTS[i], SLOTS[(i + k) % TABLES]))
            order.append(b * (b - 1) // 2 + a)
    return order


def dlrm_tower(nc, dense_ctx, ids, onehot_ids, smalls, tables, W1, b1, W2, b2, W3, out):
    fp32 = mybir.dt.float32
    fp32r = mybir.dt.float32r
    i32 = mybir.dt.int32
    ALU = mybir.AluOpType
    ACT = mybir.ActivationFunctionType

    P = 128
    TILES = BATCH // P
    SLOT = 32
    QUADS = P // SLOT
    EACH = P // QUADS
    GROUP = 4
    NGATHER, NHOT = len(GATHER), len(ONEHOT)
    GROUPS = [list(range(f, min(f + GROUP, NGATHER))) for f in range(0, NGATHER, GROUP)]
    NG = len(GROUPS)
    RING = 3
    HOTS = 3
    BY_DVE = 7
    BY_ACT = CHUNKS - BY_DVE
    ROW_TILES = 2
    PER_BANK = EACH // 2
    REACH = (TABLES - 1) // 2
    KC = (PAIRS + DENSE + 1 + P - 1) // P
    KLAST = PAIRS + DENSE + 1 - (KC - 1) * P
    U1, U2 = H1 // P, H2 // P

    ctx = ExitStack()
    with ctx:
        def sb(name, shape, dt=fp32):
            return ctx.enter_context(nc.sbuf_tensor(name, shape, dt))

        def ps(name, shape):
            return ctx.enter_context(nc.psum_tensor(name, shape, fp32))

        def sem(name):
            return ctx.enter_context(nc.semaphore(name))

        idx = sb("idx", [P, TILES, TABLES], i32)
        rows = sb("rows", [P, ROW_TILES, NGATHER, DIM])
        spread = sb("spread", [P, RING, BATCH], i32)
        rowI = sb("rowI", [P, CHUNKS], i32)
        row_no = sb("row_no", [P, CHUNKS])
        row_neg = sb("row_neg", [P, CHUNKS])
        small = sb("small", [P, RING, CHUNKS, DIM])
        high = sb("high", [P, 2, CHUNKS, DIM], fp32r)
        low = sb("low", [P, 2, CHUNKS, DIM], fp32r)
        hot_dve = sb("hot_dve", [P, HOTS, BY_DVE, BATCH], fp32r)
        hot_act = sb("hot_act", [P, HOTS, BY_ACT, BATCH], fp32r)
        away = sb("away", [P, BY_ACT, BATCH])
        cols = sb("cols", [P, BATCH, SLOT])
        ident = sb("ident", [P, P])
        ones = sb("ones", [P, P])
        turned = sb("turned", [P, TABLES + REACH, SLOT])
        feat = sb("feat", [P, TILES, KC * P])
        featT = sb("featT", [P, KC, P])
        w1 = sb("w1", [P, KC, H1])
        w2 = sb("w2", [P, U1, H2])
        w3 = sb("w3", [P, U2])
        b2c = sb("b2c", [P, U2])
        h1 = sb("h1", [P, U1, P])
        h2 = sb("h2", [P, U2, P])
        y = sb("y", [1, BATCH])

        psT = [ps(f"psT{i}", [P, GROUP, P]) for i in range(2)]
        psG = [ps(f"psG{i}", [P, 2, 512]) for i in range(2)]
        psA = ps("psA", [P, 512])
        psH = ps("psH", [P, U1, P])
        LAST = TILES - 1

        def gram_ps(t, g):
            o = g % PER_BANK * TABLES
            return psG[t % 2][:, g // PER_BANK, o:o + TABLES]

        def feat_ps(t, c):
            return psH[:, c, :] if t < LAST or c == 0 else psG[LAST % 2][:, c - 1, 0:P]

        def h1_ps(t, u):
            return psH[:, u, :] if t < LAST else psT[u][:, 0, :] if u < 2 else psG[1 - LAST % 2][:, u - 2, 0:P]

        def h2_ps(t, u):
            return psA[:, u * P:(u + 1) * P] if t < LAST or u == 0 else psH[:, 1, :]

        psY = psA[0:1, H2:H2 + P]

        def ps_lookup(i):
            return psG[1][:, i % 2, :]

        ids_in = sem("ids_in")
        dense_in = sem("dense_in")
        w1_in = sem("w1_in")
        w2_in = sem("w2_in")
        spread_in = [sem(f"spread_in{i}") for i in range(RING)]
        small_in = [sem(f"small_in{i}") for i in range(RING)]
        row_ids = sem("row_ids")
        row_nos = sem("row_nos")
        high_made = sem("high_made")
        low_made = sem("low_made")
        hot_made_dve = sem("hot_made_dve")
        hot_made_act = sem("hot_made_act")
        away_made = sem("away_made")
        looked_up = sem("looked_up")
        lookup_kept = sem("lookup_kept")
        gathered = [sem(f"gathered{g}") for g in range(NG)]
        ones_set = sem("ones_set")
        ident_set = sem("ident_set")
        pads_set = sem("pads_set")
        group_turned = sem("group_turned")
        group_kept_dve = sem("group_kept_dve")
        group_kept_act = sem("group_kept_act")
        gram_done = sem("gram_done")
        blocks_turned = sem("blocks_turned")
        pairs_packed = sem("pairs_packed")
        feat_turned = sem("feat_turned")
        feat_kept = sem("feat_kept")
        h1_done = sem("h1_done")
        h1_kept = sem("h1_kept")
        h2_done = sem("h2_done")
        h2_kept = sem("h2_kept")
        y_done = sem("y_done")
        y_kept = sem("y_kept")
        y_out = sem("y_out")

        block = ctx.enter_context(nc.Block())

        def hot(i, c):
            return hot_dve[:, i % HOTS, c, :] if c < BY_DVE else hot_act[:, i % HOTS, c - BY_DVE, :]

        WARM = 17
        AFTER = [[], [0], [1], [2], [], [3], [4], [5], [], [6, 7]]

        def by_dve(t, g):
            return (t, g) in ((2, 2), (2, 4), (3, 1), (3, 3), (3, 4))

        def moved(dve, t, g):
            return sum(by_dve(q // NG, q % NG) == dve for q in range(t * NG + g))

        @block.sync
        def _(sp):
            sp.dma_start(idx[:, :, :], ids.rearrange("(t p) f -> p t f", p=P)).then_inc(ids_in, 16)

            def load_small(i):
                sp.dma_start(spread[:, i % RING, :], onehot_ids[i:i + 1, :].partition_broadcast(P)
                             ).then_inc(spread_in[i % RING], 16)
                sp.dma_start(small[:, i % RING, :, :], smalls[:, i, :, :]
                             ).then_inc(small_in[i % RING], 16)

            for i in range(RING):
                load_small(i)
            sp.dma_start(feat[:, :, PAIRS:PAIRS + DENSE],
                         dense_ctx.rearrange("(t p) f -> p t f", p=P)).then_inc(dense_in, 16)
            sp.dma_start(w1[:, 0:KC - 1, :],
                         W1[0:(KC - 1) * P, :].rearrange("(c p) n -> p c n", p=P)).then_inc(w1_in, 16)
            sp.dma_start(w1[0:KLAST - 1, KC - 1, :], W1[(KC - 1) * P:PAIRS + DENSE, :]).then_inc(w1_in, 16)
            sp.dma_start(w1[KLAST - 1:KLAST, KC - 1, :], b1).then_inc(w1_in, 16)
            sp.dma_start(w2[:, :, :], W2.rearrange("(c p) n -> p c n", p=P)).then_inc(w2_in, 16)
            sp.dma_start(w3[:, :], W3).then_inc(w2_in, 16)
            sp.dma_start(b2c[:, :], b2).then_inc(w2_in, 16)
            for i in range(RING, NHOT):
                sp.wait_ge(low_made, i - RING + 1)
                sp.wait_ge(hot_made_dve, (i - RING + 1) * BY_DVE)
                sp.wait_ge(hot_made_act, (i - RING + 1) * BY_ACT)
                load_small(i)
            sp.wait_ge(y_kept, TILES)
            sp.dma_start(out, y[0:1, :]).then_inc(y_out, 16)
            sp.wait_ge(y_out, 16)

        @block.gpsimd
        def _(pool):
            nc.gpsimd.memset(ones[:, :], 1.0).then_inc(ones_set, 1)
            pool.wait_ge(ones_set, 1)
            nc.gpsimd.affine_select(out=ident[:, :], in_=ones[:, :], compare_op=ALU.is_equal, fill=0.0,
                                    base=0, pattern=[[-1, P]], channel_multiplier=1).then_inc(ident_set, 1)
            nc.gpsimd.iota(rowI[:, :], pattern=[[1, CHUNKS]], base=0, channel_multiplier=CHUNKS
                           ).then_inc(row_ids, 1)
            pool.wait_ge(ids_in, 16)
            for t in range(TILES):
                for g, group in enumerate(GROUPS):
                    if t > 0:
                        pool.wait_ge(gathered[g], 16 * len(group) * t)
                    if t >= ROW_TILES:
                        pool.wait_ge(group_turned, (t - ROW_TILES) * NG + g + 1)
                    for s in group:
                        f = GATHER[s]
                        pool.indirect_dma_start(rows[:, t % ROW_TILES, s, :], None, tables[f],
                                                bass.IndirectOffsetOnAxis(ap=idx[:, t, f:f + 1], axis=0)
                                                ).then_inc(gathered[g], 16)

        @block.tensor
        def _(pe):
            def turn_group(t, g):
                group = GROUPS[g]
                pe.wait_ge(gathered[g], 16 * len(group) * (t + 1))
                last = max((q for q in range(t * NG + g) if q % NG % 2 == g % 2), default=-1)
                if last >= 0 and by_dve(last // NG, last % NG):
                    pe.wait_ge(group_kept_dve, moved(True, 0, last + 1))
                elif last >= 0:
                    pe.wait_ge(group_kept_act, moved(False, 0, last + 1))
                for i, f in enumerate(group):
                    last = nc.tensor.transpose(psT[g % 2][:, i, :], rows[:, t % ROW_TILES, f, :], ident[:, :])
                last.then_inc(group_turned, 1)

            def lookup(i):
                if i >= 2:
                    pe.wait_ge(lookup_kept, i - 1)
                pe.wait_ge(high_made, i + 1)
                for c in range(CHUNKS):
                    if c < BY_DVE:
                        pe.wait_ge(hot_made_dve, i * BY_DVE + c + 1)
                    else:
                        pe.wait_ge(hot_made_act, i * BY_ACT + c - BY_DVE + 1)
                    nc.tensor.matmul(ps_lookup(i), high[:, i % 2, c, :], hot(i, c), start=(c == 0), stop=False)
                pe.wait_ge(low_made, i + 1)
                for c in range(CHUNKS):
                    last = nc.tensor.matmul(ps_lookup(i), low[:, i % 2, c, :], hot(i, c), start=False,
                                            stop=(c == CHUNKS - 1))
                last.then_inc(looked_up, 1)

            def turn_feat(t):
                pe.wait_ge(pairs_packed, t + 1)
                if t > 0:
                    pe.wait_ge(h1_kept, U1 * t)
                for c in range(KC):
                    nc.tensor.transpose(feat_ps(t, c), feat[:, t, c * P:(c + 1) * P], ident[:, :]
                                        ).then_inc(feat_turned, 1)

            def layer1(t, units):
                for u in units:
                    for c in range(KC):
                        if u == 0:
                            pe.wait_ge(feat_kept, KC * (t + 1) if t < LAST else KC * t + c + 1)
                        k = P if c < KC - 1 else KLAST
                        last = nc.tensor.matmul(h1_ps(t, u), w1[0:k, c, u * P:(u + 1) * P], featT[0:k, c, :],
                                                start=(c == 0), stop=(c == KC - 1))
                    last.then_inc(h1_done, 1)

            def layer2(t, units):
                if t > 0:
                    pe.wait_ge(y_kept, t)
                for u in units:
                    for c in range(U1):
                        if u == 0:
                            pe.wait_ge(h1_kept, U1 * t + c + 1)
                        last = nc.tensor.matmul(h2_ps(t, u), w2[:, c, u * P:(u + 1) * P], h1[:, c, :],
                                                start=(c == 0), stop=(c == U1 - 1))
                    last.then_inc(h2_done, 1)

            def layer3(t):
                for c in range(U2):
                    pe.wait_ge(h2_kept, U2 * t + (c + 1 if t == LAST else U2))
                    last = nc.tensor.matmul(psY, w3[:, c:c + 1], h2[:, c, :], start=(c == 0), stop=(c == U2 - 1))
                last.then_inc(y_done, 1)

            def gram_products(t, first, end):
                if first == 0:
                    if t == 0:
                        pe.wait_ge(lookup_kept, NHOT)
                    if moved(True, t + 1, 0) > 0:
                        pe.wait_ge(group_kept_dve, moved(True, t + 1, 0))
                    pe.wait_ge(group_kept_act, moved(False, t + 1, 0))
                    if t >= 2:
                        pe.wait_ge(blocks_turned, 2 * (t - 1))
                for g in range(first, end):
                    for j in range(QUADS):
                        b = t * P + j * SLOT + g
                        last = nc.tensor.matmul(gram_ps(t, g)[j * SLOT:(j + 1) * SLOT, :],
                                                cols[:, b, 0:SLOT], cols[:, b, 0:TABLES], start=True, stop=True)
                if end == EACH:
                    last.then_inc(gram_done, 1)

            pe.wait_ge(ident_set, 1)
            for _ in range(WARM):
                nc.tensor.matmul(ps_lookup(1)[:, 0:P], ident[:, :], ones[:, :], start=True, stop=True)
            for i in range(NHOT):
                lookup(i)
                for q in AFTER[i]:
                    turn_group(q // NG, q % NG)
            pe.wait_ge(pads_set, 1)
            pe.wait_ge(dense_in, 16)
            pe.wait_ge(w1_in, 48)
            pe.wait_ge(w2_in, 48)
            gram_products(0, 0, 16)
            turn_group(1, 3)
            turn_group(1, 4)
            gram_products(0, 16, EACH)
            gram_products(1, 0, 4)
            turn_group(2, 0)
            gram_products(1, 4, 12)
            turn_group(2, 1)
            gram_products(1, 12, 20)
            turn_feat(0)
            gram_products(1, 20, 26)
            layer1(0, (0,))
            gram_products(1, 26, EACH)
            layer1(0, (1, 2, 3))
            turn_group(2, 2)
            turn_group(2, 3)
            layer2(0, (0,))
            turn_group(2, 4)
            layer2(0, (1,))
            gram_products(2, 0, 4)
            turn_feat(1)
            gram_products(2, 4, 10)
            layer3(0)
            layer1(1, (0,))
            gram_products(2, 10, 16)
            layer1(1, (1,))
            turn_group(3, 0)
            gram_products(2, 16, 22)
            layer1(1, (2,))
            gram_products(2, 22, 28)
            layer1(1, (3,))
            gram_products(2, 28, EACH)
            turn_group(3, 1)
            layer2(1, (0, 1))
            turn_group(3, 2)
            turn_feat(2)
            layer3(1)
            turn_group(3, 3)
            layer1(2, (0,))
            turn_group(3, 4)
            layer1(2, (1,))
            gram_products(3, 0, 10)
            layer1(2, (2,))
            gram_products(3, 10, 20)
            layer1(2, (3,))
            gram_products(3, 20, EACH)
            layer2(2, (0, 1))
            turn_feat(3)
            layer3(2)
            layer1(3, (0, 1, 2, 3))
            layer2(3, (0, 1))
            layer3(3)

        def group_cols(t, g):
            group = GROUPS[g]
            return cols[:, t * P:(t + 1) * P, group[0]:group[0] + len(group)]

        def group_ps(g):
            return psT[g % 2][:, 0:len(GROUPS[g]), :].rearrange("p f b -> p b f")

        def blocks(t, m):
            return psG[t % 2][:, :, 0:PER_BANK * TABLES].rearrange(
                "p a (g m) -> p m a g", g=PER_BANK)[:, 0:m, :, :]

        @block.vector
        def _(dve):
            nc.vector.memset(cols[:, :, TABLES:SLOT], 0.0)
            nc.vector.memset(feat[:, :, PAIRS + DENSE:PAIRS + DENSE + 1], 1.0)
            nc.vector.memset(feat[:, :, PAIRS + DENSE + 1:KC * P], 0.0).then_inc(pads_set, 1)

            def keep_group(t, g):
                dve.wait_ge(group_turned, t * NG + g + 1)
                nc.vector.tensor_copy(group_cols(t, g), group_ps(g)).then_inc(group_kept_dve, 1)

            def turn_blocks(t):
                dve.wait_ge(gram_done, t + 1)
                if t > 0:
                    dve.wait_ge(pairs_packed, t)
                nc.vector.transpose(turned[:, 0:TABLES, :].rearrange("p m n -> p (m n)"), blocks(t, TABLES)
                                    ).then_inc(blocks_turned, 1)
                nc.vector.transpose(turned[:, TABLES:TABLES + REACH, :].rearrange("p m n -> p (m n)"),
                                    blocks(t, REACH)).then_inc(blocks_turned, 1)

            def keep_feat(t):
                if t > 0:
                    dve.wait_ge(h1_done, U1 * t)
                if t < LAST:
                    dve.wait_ge(feat_turned, KC * (t + 1))
                    nc.vector.tensor_copy(featT[:, :, :], psH[:, 0:KC, :]).then_inc(feat_kept, KC)
                else:
                    for c in range(KC):
                        dve.wait_ge(feat_turned, KC * t + c + 1)
                        nc.vector.tensor_copy(featT[:, c, :], feat_ps(t, c)).then_inc(feat_kept, 1)

            def keep_y(t):
                dve.wait_ge(y_done, t + 1)
                nc.vector.tensor_copy(y[0:1, t * P:(t + 1) * P], psY).then_inc(y_kept, 1)

            def split_low(i):
                dve.wait_ge(high_made, i + 1)
                if i >= 2:
                    dve.wait_ge(looked_up, i - 1)
                nc.vector.tensor_tensor(low[:, i % 2, :, :], small[:, i % RING, :, :],
                                        high[:, i % 2, :, :].bitcast(fp32), ALU.subtract
                                        ).then_inc(low_made, 1)

            def make_hot(i):
                dve.wait_ge(spread_in[i % RING], 16 * (i // RING + 1))
                if i >= HOTS:
                    dve.wait_ge(looked_up, i - HOTS + 1)
                for c in range(BY_DVE):
                    nc.vector.tensor_scalar(hot_dve[:, i % HOTS, c, :], spread[:, i % RING, :], row_no[:, c:c + 1],
                                            None, ALU.is_equal).then_inc(hot_made_dve, 1)

            dve.wait_ge(row_ids, 1)
            nc.vector.tensor_copy(row_no[:, :], rowI[:, :])
            nc.vector.tensor_scalar(row_neg[:, :], rowI[:, :], -1.0, None, ALU.mult).then_inc(row_nos, 1)
            dve.wait_ge(row_nos, 1)
            make_hot(0)
            split_low(0)
            for i in range(NHOT):
                if i + 1 < NHOT:
                    make_hot(i + 1)
                    split_low(i + 1)
                for q in AFTER[i]:
                    if by_dve(q // NG, q % NG):
                        keep_group(q // NG, q % NG)
            turn_blocks(0)
            keep_feat(0)
            turn_blocks(1)
            keep_group(2, 2)
            keep_group(2, 4)
            keep_feat(1)
            keep_y(0)
            turn_blocks(2)
            keep_group(3, 1)
            keep_feat(2)
            keep_y(1)
            keep_group(3, 3)
            keep_group(3, 4)
            turn_blocks(3)
            keep_feat(3)
            keep_y(2)
            keep_y(3)

        @block.scalar
        def _(act):
            def keep_group(t, g):
                act.wait_ge(group_turned, t * NG + g + 1)
                nc.scalar.copy(group_cols(t, g), group_ps(g)).then_inc(group_kept_act, 1)

            def pack_pairs(t):
                ring = turned[:, :, :].rearrange("p m n -> p (m n)")
                pairs = feat[:, t, 0:PAIRS].rearrange("p (k i) -> p k i", k=REACH)
                for half, (first, end) in enumerate(((0, TABLES - REACH), (TABLES - REACH, TABLES))):
                    act.wait_ge(blocks_turned, 2 * t + half + 1)
                    src = bass.AP(ring.tensor, ring.offset + SLOT + first * (SLOT + 1),
                                  [ring.ap[0], [SLOT, REACH], [SLOT + 1, end - first]])
                    last = nc.scalar.copy(pairs[:, :, first:end], src)
                last.then_inc(pairs_packed, 1)

            def keep_h1(t):
                if t > 0:
                    act.wait_ge(h2_done, U2 * t)
                if t < LAST:
                    act.wait_ge(h1_done, U1 * (t + 1))
                    nc.scalar.activation(h1[:, :, :], psH[:, :, :], ACT.Relu).then_inc(h1_kept, U1)
                else:
                    for u in range(U1):
                        act.wait_ge(h1_done, U1 * t + u + 1)
                        nc.scalar.activation(h1[:, u, :], h1_ps(t, u), ACT.Relu).then_inc(h1_kept, 1)

            def keep_h2(t):
                if t > 0:
                    act.wait_ge(y_done, t)
                for u in range(U2):
                    act.wait_ge(h2_done, U2 * t + (u + 1 if t == LAST else U2))
                    nc.scalar.activation(h2[:, u, :], h2_ps(t, u), ACT.Relu, bias=b2c[:, u:u + 1]
                                         ).then_inc(h2_kept, 1)

            def split_high(i):
                act.wait_ge(small_in[i % RING], 16 * (i // RING + 1))
                if i >= 2:
                    act.wait_ge(looked_up, i - 1)
                nc.scalar.copy(high[:, i % 2, :, :], small[:, i % RING, :, :]).then_inc(high_made, 1)

            def make_hot(i):
                act.wait_ge(spread_in[i % RING], 16 * (i // RING + 1))
                if i > 0:
                    act.wait_ge(hot_made_act, i * BY_ACT)
                for c in range(BY_ACT):
                    nc.scalar.activation(away[:, c, :], spread[:, i % RING, :], ACT.Abs,
                                         bias=row_neg[:, BY_DVE + c:BY_DVE + c + 1]).then_inc(away_made, 1)
                if i >= HOTS:
                    act.wait_ge(looked_up, i - HOTS + 1)
                for c in range(BY_ACT):
                    act.wait_ge(away_made, i * BY_ACT + c + 1)
                    nc.scalar.activation(hot_act[:, i % HOTS, c, :], away[:, c, :], ACT.Relu, bias=1.0, scale=-1.0
                                         ).then_inc(hot_made_act, 1)

            def keep_lookup(i):
                act.wait_ge(looked_up, i + 1)
                nc.scalar.copy(cols[:, :, NGATHER + i], ps_lookup(i)).then_inc(lookup_kept, 1)

            act.wait_ge(ones_set, 1)
            nc.scalar.activation(h1[0:1, 0, :], ones[0:1, :], ACT.Abs)
            act.wait_ge(row_nos, 1)
            make_hot(0)
            split_high(0)
            for i in range(NHOT):
                if i + 1 < NHOT:
                    make_hot(i + 1)
                    split_high(i + 1)
                keep_lookup(i)
                for q in AFTER[i]:
                    if not by_dve(q // NG, q % NG):
                        keep_group(q // NG, q % NG)
            keep_group(1, 3)
            keep_group(1, 4)
            keep_group(2, 0)
            pack_pairs(0)
            keep_group(2, 1)
            pack_pairs(1)
            keep_h1(0)
            keep_group(2, 3)
            act.wait_ge(w2_in, 48)
            keep_h2(0)
            keep_group(3, 0)
            keep_h1(1)
            pack_pairs(2)
            keep_h2(1)
            keep_group(3, 2)
            keep_h1(2)
            pack_pairs(3)
            keep_h2(2)
            keep_h1(3)
            keep_h2(3)


def kernel(**inputs):
    import numpy as np
    import concourse.bacc as bacc
    from concourse.bass_utils import run_bass_kernel_spmd

    nc = bacc.Bacc("TRN2", target_bir_lowering=False, num_devices=1)
    arrays = {}

    def given(name, a):
        arrays[name] = np.ascontiguousarray(a)
        return nc.dram_tensor(name, arrays[name].shape, mybir.dt.from_np(arrays[name].dtype),
                              kind="ExternalInput").ap()

    w = np.asarray(inputs["W_top1"])
    w = np.concatenate([w[np.array(pair_rows())], w[PAIRS:]], axis=0)
    ids = np.asarray(inputs["ids"])
    smalls = np.zeros((len(ONEHOT), 128 * CHUNKS, DIM), np.float32)
    for i, f in enumerate(ONEHOT):
        smalls[i, :len(inputs[f"tbl_{f}"])] = inputs[f"tbl_{f}"]
    smalls = smalls.reshape(len(ONEHOT), 128, CHUNKS, DIM).transpose(1, 0, 2, 3)
    args = [given("dense_dram", inputs["dense_ctx"]), given("ids_dram", ids),
            given("onehot_ids_dram", ids[:, ONEHOT].T),
            given("smalls_dram", smalls),
            [given(f"table{f}_dram", inputs[f"tbl_{f}"]) if f in GATHER else None for f in range(TABLES)],
            given("w1_dram", w), given("b1_dram", np.asarray(inputs["b_top1"]).reshape(1, H1)),
            given("w2_dram", inputs["W_top2"]),
            given("b2_dram", np.asarray(inputs["b_top2"]).reshape(H2 // 128, 128).T),
            given("w3_dram", np.asarray(inputs["W_top3"]).reshape(H2 // 128, 128).T)]
    out = nc.dram_tensor("y_dram", (1, BATCH), mybir.dt.float32, kind="ExternalOutput").ap()
    dlrm_tower(nc, *args, out)
    r = run_bass_kernel_spmd(nc, [arrays], core_ids=[0])
    return r.results[0]["y_dram"].reshape(BATCH, 1)
```
